# Optimizing a Trainium2 kernel written in Bass

```python
import numpy as np
import jax
import jax.numpy as jnp

def _softmax(x, axis=-1):
    return jax.nn.softmax(x, axis=axis)

def _gelu(x):
    return jax.nn.gelu(x, approximate=True)

def _silu(x):
    return jax.nn.silu(x)

def _sigmoid(x):
    return jax.nn.sigmoid(x)

def _layernorm(x, axis=-1, eps=1e-05):
    m = jnp.mean(x, axis=axis, keepdims=True)
    v = jnp.var(x, axis=axis, keepdims=True)
    return (x - m) / jnp.sqrt(v + eps)

def _scatter_add(tgt, idx, src, axis=0):
    return tgt.at[idx].add(src)

def _segment_sum(src, seg, n):
    return jax.ops.segment_sum(src, seg, n)
kernel_name = 'mk_adaln_d1_jaxref_r8_4f4051'

def setup_inputs(seed: int=0):
    np.random.seed(seed)
    _w = jnp.asarray

    def _L0_attn_setup():
        import jax, jax.numpy as jnp
        import numpy as np
        DIM = 256
        NUM_HEADS = 16
        HEAD_DIM = DIM // NUM_HEADS
        WINDOW_SIZE = 384
        SCALE = HEAD_DIM ** (-0.5)
        NEG_INF = -1000000000.0

        def _window_mask(q_len: int, kv_len: int) -> jnp.ndarray:
            i = jnp.arange(q_len)[:, None]
            j = jnp.arange(kv_len)[None, :]
            start = jnp.maximum(0, kv_len - WINDOW_SIZE + i)
            allowed = (j >= start) & (j <= i)
            return ~allowed
        key = jax.random.key(seed)
        ks = jax.random.split(key, 6)
        B, N = (2, 256)
        x = jax.random.normal(ks[0], (B, N, DIM), dtype=jnp.float32)
        w_init = 0.02
        Wq = jax.random.normal(ks[1], (DIM, DIM), dtype=jnp.float32) * w_init
        Wk = jax.random.normal(ks[2], (DIM, DIM), dtype=jnp.float32) * w_init
        Wv = jax.random.normal(ks[3], (DIM, DIM), dtype=jnp.float32) * w_init
        Wo = jax.random.normal(ks[4], (DIM, DIM), dtype=jnp.float32) * w_init
        zeros = jnp.zeros((DIM,), dtype=jnp.float32)
        return {'x': x, 'Wq': Wq, 'bq': zeros, 'Wk': Wk, 'bk': zeros, 'Wv': Wv, 'bv': zeros, 'Wo': Wo, 'bo': zeros}
    _L0_attn_in = _L0_attn_setup()

    def _L0_ffn_setup():
        import jax, jax.numpy as jnp
        import numpy as np
        E, TOPK, H, I, NSH = (8, 2, 256, 640, 2)
        B, S = (2, 128)
        key = jax.random.key(seed)
        ks = jax.random.split(key, 8)
        sc = 0.02
        return {'x': jax.random.normal(ks[0], (B, S, H), dtype=jnp.float32), 'w_router': jax.random.normal(ks[1], (E, H), dtype=jnp.float32), 'wg': jax.random.normal(ks[2], (E, I, H), dtype=jnp.float32) * sc, 'wu': jax.random.normal(ks[3], (E, I, H), dtype=jnp.float32) * sc, 'wd': jax.random.normal(ks[4], (E, H, I), dtype=jnp.float32) * sc, 'sg': jax.random.normal(ks[5], (NSH, I, H), dtype=jnp.float32) * sc, 'su': jax.random.normal(ks[6], (NSH, I, H), dtype=jnp.float32) * sc, 'sd': jax.random.normal(ks[7], (NSH, H, I), dtype=jnp.float32) * sc}
    _L0_ffn_in = _L0_ffn_setup()
    _L0_c = _w((lambda *s: np.random.randn(*s).astype(np.float32) * 0.05)(4, 256))
    _L0_wmod = _w((lambda *s: np.random.randn(*s).astype(np.float32) * 0.05)(256, 6 * 256) * 256 ** (-0.5))
    _d = {'L0_attn_x': _L0_attn_in['x'], 'L0_attn_Wq': _L0_attn_in['Wq'], 'L0_attn_bq': _L0_attn_in['bq'], 'L0_attn_Wk': _L0_attn_in['Wk'], 'L0_attn_bk': _L0_attn_in['bk'], 'L0_attn_Wv': _L0_attn_in['Wv'], 'L0_attn_bv': _L0_attn_in['bv'], 'L0_attn_Wo': _L0_attn_in['Wo'], 'L0_attn_bo': _L0_attn_in['bo'], 'L0_ffn_w_router': _L0_ffn_in['w_router'], 'L0_ffn_wg': _L0_ffn_in['wg'], 'L0_ffn_wu': _L0_ffn_in['wu'], 'L0_ffn_wd': _L0_ffn_in['wd'], 'L0_ffn_sg': _L0_ffn_in['sg'], 'L0_ffn_su': _L0_ffn_in['su'], 'L0_ffn_sd': _L0_ffn_in['sd'], 'L0_c': _L0_c, 'L0_wmod': _L0_wmod}
    _x0 = _d['L0_attn_x']
    _d['L0_attn_x'] = jax.random.normal(jax.random.fold_in(jax.random.key(seed), 1), (4, 256, 256), dtype=_x0.dtype)
    del _x0
    return _d

def reference(L0_attn_x, L0_attn_Wq, L0_attn_bq, L0_attn_Wk, L0_attn_bk, L0_attn_Wv, L0_attn_bv, L0_attn_Wo, L0_attn_bo, L0_ffn_w_router, L0_ffn_wg, L0_ffn_wu, L0_ffn_wd, L0_ffn_sg, L0_ffn_su, L0_ffn_sd, L0_c, L0_wmod):

    def _L0_attn_ref(x, Wq, bq, Wk, bk, Wv, bv, Wo, bo):
        import jax, jax.numpy as jnp
        import numpy as np
        DIM = 256
        NUM_HEADS = 16
        HEAD_DIM = DIM // NUM_HEADS
        WINDOW_SIZE = 384
        SCALE = HEAD_DIM ** (-0.5)
        NEG_INF = -1000000000.0

        def _window_mask(q_len: int, kv_len: int) -> jnp.ndarray:
            i = jnp.arange(q_len)[:, None]
            j = jnp.arange(kv_len)[None, :]
            start = jnp.maximum(0, kv_len - WINDOW_SIZE + i)
            allowed = (j >= start) & (j <= i)
            return ~allowed
        B, N, C = x.shape
        H, D = (NUM_HEADS, HEAD_DIM)
        q = (x @ Wq.T + bq).reshape(B, N, H, D).transpose(0, 2, 1, 3)
        k = (x @ Wk.T + bk).reshape(B, N, H, D).transpose(0, 2, 1, 3)
        v = (x @ Wv.T + bv).reshape(B, N, H, D).transpose(0, 2, 1, 3)
        scores = jnp.einsum('bhqd,bhkd->bhqk', q, k) * SCALE
        mask = _window_mask(N, N)
        scores = jnp.where(mask[None, None], NEG_INF, scores)
        attn = jax.nn.softmax(scores, axis=-1)
        out = jnp.einsum('bhqk,bhkd->bhqd', attn, v)
        out = out.transpose(0, 2, 1, 3).reshape(B, N, C)
        return out @ Wo.T + bo

    def _L0_ffn_ref(x, w_router, wg, wu, wd, sg, su, sd):
        import jax, jax.numpy as jnp
        import numpy as np
        E, TOPK, H, I, NSH = (8, 2, 256, 640, 2)
        B, S = (2, 128)
        b, s, h = x.shape
        xt = x.reshape(-1, h)
        T = xt.shape[0]
        logits = jnp.einsum('th,eh->te', xt.astype(jnp.float32), w_router.astype(jnp.float32))
        scores = jax.nn.sigmoid(logits)
        topk_w, topk_i = jax.lax.top_k(scores, TOPK)
        topk_w = topk_w / jnp.sum(topk_w, axis=-1, keepdims=True)
        comb = jnp.zeros((T, E), dtype=xt.dtype)
        comb = comb.at[jnp.arange(T)[:, None], topk_i].add(topk_w.astype(xt.dtype))
        gate = jax.nn.silu(jnp.einsum('th,eih->tei', xt, wg))
        up = jnp.einsum('th,eih->tei', xt, wu)
        expert_out = jnp.einsum('tei,ehi->teh', gate * up, wd)
        out = jnp.einsum('te,teh->th', comb, expert_out)
        sgate = jax.nn.silu(jnp.einsum('th,jih->tji', xt, sg))
        sup = jnp.einsum('th,jih->tji', xt, su)
        out = out + jnp.einsum('tji,jhi->th', sgate * sup, sd)
        return out.reshape(b, s, h)
    x = L0_attn_x
    mod = (_silu(L0_c) @ L0_wmod).reshape(L0_c.shape[0], 6, 1, -1)
    sa, ca, ga, sb, cb, gb = (mod[:, 0], mod[:, 1], mod[:, 2], mod[:, 3], mod[:, 4], mod[:, 5])
    ga = (2 * (ga >= 0) - 1) * jnp.maximum(jnp.abs(ga), 0.25)
    gb = (2 * (gb >= 0) - 1) * jnp.maximum(jnp.abs(gb), 0.25)
    h = _layernorm(x, axis=-1) * (1 + ca) + sa
    x = x + ga * _L0_attn_ref(h, L0_attn_Wq, L0_attn_bq, L0_attn_Wk, L0_attn_bk, L0_attn_Wv, L0_attn_bv, L0_attn_Wo, L0_attn_bo)
    h = _layernorm(x, axis=-1) * (1 + cb) + sb
    x = x + gb * _L0_ffn_ref(h, L0_ffn_w_router, L0_ffn_wg, L0_ffn_wu, L0_ffn_wd, L0_ffn_sg, L0_ffn_su, L0_ffn_sd)
    return x

_drawn_inputs = setup_inputs


def setup_inputs(seed=0):
    import zlib

    import numpy as np

    out = dict(_drawn_inputs(seed))
    spreads = {'L0_attn_bq': (0.0, 0.8),
     'L0_attn_bk': (0.0, 0.8),
     'L0_attn_bv': (0.0, 0.8),
     'L0_attn_bo': (0.0, 0.331)}
    factors = {'L0_attn_Wq': 8.0,
     'L0_attn_Wk': 8.0,
     'L0_attn_Wv': 8.0,
     'L0_attn_Wo': 6.371,
     'L0_ffn_w_router': 8.0,
     'L0_ffn_wg': 8.0,
     'L0_ffn_wu': 8.0,
     'L0_ffn_wd': 8.0,
     'L0_ffn_sg': 6.048,
     'L0_ffn_su': 5.98,
     'L0_ffn_sd': 5.981}
    for name, (base, spread) in spreads.items():
        noise = np.random.default_rng([zlib.crc32(name.encode()), seed]).standard_normal(out[name].shape)
        drawn = base * np.exp(spread * noise) if base else spread * noise
        out[name] = jnp.asarray(drawn.astype(out[name].dtype))
    for name, factor in factors.items():
        out[name] = (out[name] * factor).astype(out[name].dtype)
    return out
```

```python
import concourse.bass as bass
from concourse import mybir
from contextlib import ExitStack

B, N, C = 4, 256, 256
H, D = 16, 16
P = 128
T = B * N
NT = T // P
TB = N // P
KC = C // P
GH = 4
G = H // GH
E, NSH, I = 8, 2, 640
IT = I // P
TC = 512
NCH = T // TC
SCALE = float(D) ** -0.5
NEG_INF = -1.0e9
EPS = 1e-5
SA, CA, GA, SB, CB, GB = range(6)
UW = KC * I
DW = IT * C
W1 = 2 * UW + DW
UN = 2 * B
HD = D + 1
VS = (H - 1) * HD + P
STR = P // GH
FLOOR = -3.0e38
RSTEPS = 19
EXP_MAX = 87.0


def adaln_block_kernel(nc, x, c_t, wmod, wqk, bqk, low_rows, wv, bv, wo, bo, wr, experts, out):
    fp32 = mybir.dt.float32
    f32r = mybir.dt.float32r
    bf16 = mybir.dt.bfloat16
    ALU = mybir.AluOpType
    ACT = mybir.ActivationFunctionType
    AX = mybir.AxisListType
    ds = bass.ds

    x_tiles = x.rearrange("(n p) c -> p n c", p=P)
    out_tiles = out.rearrange("(n p) c -> p n c", p=P)

    ctx = ExitStack()
    with ctx:
        def sb(name, shape, dt=fp32, where=ctx):
            return where.enter_context(nc.sbuf_tensor(name, shape, dt))

        def sem(name):
            return ctx.enter_context(nc.semaphore(name))

        ident = sb("ident", [P, P])
        mask = sb("mask", [P, 3 * P])
        sel = sb("sel", [E, E, P])
        zeros = sb("zeros", [P, 512], bf16)
        half = sb("half", [P, TB])
        x_sb = sb("x_sb", [P, NT, C])
        mod_sb = sb("mod_sb", [P, 4, KC, B])
        gb_b = sb("gb_b", [P, B, C])
        stats = sb("stats", [P, NT, 6])
        mv = sb("mv", [P, NT, 2])
        var_eps = sb("var_eps", [P, NT])
        rstd = sb("rstd", [P, NT])
        h_hi = sb("h_hi", [P, KC, T], f32r)
        h_lo = sb("h_lo", [P, KC, T], f32r)
        wr_sb = sb("wr_sb", [P, KC, P])
        wr_hi = sb("wr_hi", [P, KC, P], f32r)
        wr_lo = sb("wr_lo", [P, KC, P], f32r)
        lg_t = sb("lg_t", [E, T])
        cand = sb("cand", [P, NT, E])
        rt = {n: sb("r_" + n, [P, NT, E]) for n in ("z", "e", "p", "s", "eq1", "t1", "m1", "s2", "eq2", "t2", "m2", "m", "c")}
        rv = {n: sb("r_" + n, [P, NT]) for n in ("v1", "i1", "v2", "i2", "den", "rden")}
        comb = sb("comb", [P, NT, E])
        comb_t = sb("comb_t", [E, T])
        res = sb("res", [P, 2, C])

        a1 = ExitStack()
        wmod_sb = sb("wmod_sb", [P, KC, 6 * C], where=a1)
        ct_sb = sb("ct_sb", [P, KC, B], where=a1)
        sc_sb = sb("sc_sb", [P, KC, B], where=a1)
        gate_rows = sb("gate_rows", [B, 2 * C], where=a1)
        gate_abs = sb("gate_abs", [B, 2 * C], where=a1)
        gate_sign = sb("gate_sign", [B, 2 * C], where=a1)
        gate_fin = sb("gate_fin", [B, 2 * C], where=a1)
        wv_raw = sb("wv_raw", [P, KC, C], where=a1)
        wv_hi = sb("wv_hi", [P, KC, C], f32r, where=a1)
        wv_lo = sb("wv_lo", [P, KC, C], f32r, where=a1)
        bv_b = sb("bv_b", [P, C], where=a1)
        wqk_raw = sb("wqk_raw", [P, G, 2 * KC * P], where=a1)
        bqk_sb = sb("bqk_sb", [P, 3, G], where=a1)
        low_sb = sb("low_sb", [P, 1], where=a1)
        v_sb = sb("v_sb", [P, NT, VS], where=a1)
        wqk_hi = sb("wqk_hi", [P, 2 * KC * P], f32r, where=a1)
        wqk_lo = sb("wqk_lo", [P, 2 * KC * P], f32r, where=a1)
        q_sub = sb("q_sub", [P, T], f32r, where=a1)
        q_st = sb("q_st", [P, T], f32r, where=a1)
        k_hi = sb("k_hi", [P, T], f32r, where=a1)
        k_lo = sb("k_lo", [P, T], f32r, where=a1)
        kd_hi = sb("kd_hi", [P, GH, T], f32r, where=a1)
        kd_lo = sb("kd_lo", [P, GH, T], f32r, where=a1)
        SR, TR = 4, 2
        p_sb = sb("p_sb", [P, SR, 6 * P], where=a1)
        rmax = sb("rmax", [P, SR, 4], where=a1)
        nmax = sb("nmax", [P, SR, 4], where=a1)
        p_t = sb("p_t", [P, TR, 6 * P], where=a1)
        rsum = sb("rsum", [P, TR, 4], where=a1)
        a1.close()
        w_raw = sb("w_raw", [P, W1])
        w_hi = sb("w_hi", [P, 2, W1], f32r)
        w_lo = sb("w_lo", [P, 2, W1], f32r)
        comb_b = sb("comb_b", [P, E, T])

        a2 = ExitStack()
        xn = sb("xn", [P, NT, C], where=a2)
        h_full = sb("h_full", [P, 2, KC, N], where=a2)
        ga_b = sb("ga_b", [P, B, C], where=a2)
        attn = sb("attn", [P, NT, C], where=a2)
        wo_raw = sb("wo_raw", [P, KC, C], where=a2)
        wo_hi = sb("wo_hi", [P, KC, C], f32r, where=a2)
        wo_lo = sb("wo_lo", [P, KC, C], f32r, where=a2)
        bo_b = sb("bo_b", [P, C], where=a2)
        ot_hi = sb("ot_hi", [P, 2, KC * P], f32r, where=a2)
        ot_lo = sb("ot_lo", [P, 2, KC * P], f32r, where=a2)
        y_sb = sb("y_sb", [P, 2, C], where=a2)
        y_gated = sb("y_gated", [P, 2, C], where=a2)
        a2.close()
        silu_sb = sb("silu_sb", [P, 2, TC])
        act_u = sb("act_u", [P, 2, TC])
        act_f = sb("act_f", [P, 2, TC])
        act_hi = sb("act_hi", [P, 2, TC], f32r)
        act_lo = sb("act_lo", [P, 2, TC], f32r)

        ps = ctx.enter_context(nc.psum_tensor("ps", [P, 8, 512], fp32))

        s_xload = [sem(f"s_xload{b}") for b in range(B)]
        s_small = sem("s_small")
        s_wmod = sem("s_wmod")
        s_wvl = sem("s_wvl")
        s_wqkl = sem("s_wqkl")
        s_wol = sem("s_wol")
        s_const = sem("s_const")
        s_pstep = sem("s_pstep")
        s_sc = sem("s_sc")
        s_modp = sem("s_modp")
        s_mod = sem("s_mod")
        s_gstep = sem("s_gstep")
        s_gbp = sem("s_gbp")
        s_gb = sem("s_gb")
        s_st = sem("s_st")
        s_mv = sem("s_mv")
        s_rstd = sem("s_rstd")
        s_xn = sem("s_xn")
        s_xt = sem("s_xt")
        s_hhi = sem("s_hhi")
        s_hful = sem("s_hful")
        s_hlo = sem("s_hlo")
        s_wvs = sem("s_wvs")
        s_wos = sem("s_wos")
        s_vp = sem("s_vp")
        s_v = sem("s_v")
        s_wqkh = sem("s_wqkh")
        s_wqks = sem("s_wqks")
        s_projq = sem("s_projq")
        s_projk = sem("s_projk")
        s_qsub = sem("s_qsub")
        s_khi = sem("s_khi")
        s_q = sem("s_q")
        s_k = sem("s_k")
        s_kd = sem("s_kd")
        s_wrs = sem("s_wrs")
        s_lgt = sem("s_lgt")
        s_lgs = sem("s_lgs")
        s_own = sem("s_own")
        s_s = sem("s_s")
        s_ttr = sem("s_ttr")
        s_nm = sem("s_nm")
        s_exp = sem("s_exp")
        s_t = sem("s_t")
        s_pta = sem("s_pta")
        s_ptv = sem("s_ptv")
        s_pv = sem("s_pv")
        s_rs = sem("s_rs")
        s_at = sem("s_at")
        s_ot = sem("s_ot")
        s_oth = sem("s_oth")
        s_otl = sem("s_otl")
        s_y = sem("s_y")
        s_yb = sem("s_yb")
        s_yg = sem("s_yg")
        s_x2 = sem("s_x2")
        s_lg = sem("s_lg")
        s_rstep = sem("s_rstep")
        s_re = sem("s_re")
        s_ct = sem("s_ct")
        s_cts = sem("s_cts")
        s_cb = sem("s_cb")
        s_cbs = sem("s_cbs")
        s_wl = sem("s_wl")
        s_wh = sem("s_wh")
        s_ws = sem("s_ws")
        s_gu = sem("s_gu")
        s_silu = sem("s_silu")
        s_au = sem("s_au")
        s_af = sem("s_af")
        s_ah = sem("s_ah")
        s_al = sem("s_al")
        s_dn = sem("s_dn")
        s_acc0 = sem("s_acc0")
        s_fin = sem("s_fin")
        s_res = sem("s_res")
        s_resg = sem("s_resg")
        s_out = [sem(f"s_out{i}") for i in range(2)]

        UE = NCH * IT
        EA = E + NSH
        PARTS = [(0, UW), (UW, 2 * UW), (2 * UW, W1)]
        QB = (0, 2 * P)

        block = ctx.enter_context(nc.Block())

        @block.sync
        def _(sp):
            for b in range(B):
                sp.dma_start(x_sb[:, TB * b:TB * b + TB, :], x_tiles[:, TB * b:TB * b + TB, :]).then_inc(s_xload[b], 16)
            sp.dma_start(wv_raw[:, :, :], wv).then_inc(s_wvl, 16)
            sp.dma_start(wqk_raw[:, :, :], wqk).then_inc(s_wqkl, 16)
            sp.dma_start(wo_raw[:, :, :], wo).then_inc(s_wol, 16)
            sp.sem_inc(s_kd, 16)
            sp.wait_ge(s_const, 9)
            with sp.Fori(0, G) as g:
                for src, dst, done in ((k_hi, kd_hi, s_khi), (k_lo, kd_lo, s_k)):
                    sp.wait_ge(done, g + 1)
                    for r in range(GH):
                        sp.dma_start(dst[STR * r:STR * r + STR, r, :].bitcast(fp32), src[STR * r:STR * r + STR, :].bitcast(fp32)).then_inc(s_kd, 16)
            sp.wait_ge(s_at, 2 + G * UN)
            sp.dma_start(w_raw[:, :], experts[0]).then_inc(s_wl, 16)
            with sp.Fori(1, EA) as e:
                parts = sp.snap(e * 3)
                sp.wait_ge(s_kd, 16)
                sp.wait_ge(s_wh, parts)
                sp.wait_ge(s_ws, parts)
                sp.dma_start(w_raw[:, :], experts[ds(e, 1)].rearrange("a p w -> (a p) w")).then_inc(s_wl, 16)
            for n in range(NT):
                sp.wait_ge(s_res, n + 1)
                sp.dma_start(out_tiles[:, n, :], res[:, n % 2, :]).then_inc(s_out[n % 2], 16)
            for i in range(2):
                sp.wait_ge(s_out[i], 16 * (NT // 2))

        @block.gpsimd
        def _(pool):
            pool.memset(ident[:, :], 0.0).then_inc(s_pstep, 1)
            pool.memset(sel[:, :, :], 0.0).then_inc(s_pstep, 1)
            pool.memset(mask[:, :], 0.0).then_inc(s_pstep, 1)
            pool.memset(v_sb[:, :, :], 0.0).then_inc(s_pstep, 1)
            pool.memset(half[:, :], -0.5).then_inc(s_const, 1)
            pool.memset(zeros[:, :], 0.0).then_inc(s_const, 1)
            pool.wait_ge(s_pstep, 4)
            pool.affine_select(out=ident[:, :], in_=ident[:, :], compare_op=ALU.not_equal, fill=1.0,
                               base=0, pattern=[[-1, P]], channel_multiplier=1).then_inc(s_const, 1)
            pool.affine_select(out=sel[:, :, :], in_=sel[:, :, :], compare_op=ALU.not_equal, fill=1.0,
                               base=0, pattern=[[-1, E], [0, P]], channel_multiplier=1).then_inc(s_const, 1)
            for blk, sign in ((0, 1), (1, -1), (2, 1)):
                m = mask[:, blk * P:(blk + 1) * P]
                pool.affine_select(out=m, in_=m, compare_op=ALU.is_ge, fill=NEG_INF / SCALE,
                                   base=0, pattern=[[-sign, P]], channel_multiplier=sign).then_inc(s_const, 1)
            pool.memset(kd_hi[:, :, :].bitcast(fp32), 0.0).then_inc(s_const, 1)
            pool.memset(kd_lo[:, :, :].bitcast(fp32), 0.0).then_inc(s_const, 1)
            ones = v_sb[:, :, 0:H * HD].rearrange("p n (h d) -> p n h d", d=HD)[:, :, :, D:HD]
            pool.memset(ones, 1.0).then_inc(s_const, 1)
            pool.iota(cand[:, :, :], pattern=[[0, NT], [1, E]], base=-E, channel_multiplier=0,
                      allow_small_or_imprecise_dtypes=True).then_inc(s_const, 1)
            for k in range(2 * B):
                b = k % B
                t = slice(TB * b, TB * b + TB)
                pool.wait_ge(s_mv, TB * (k + 1))
                pool.tensor_scalar(var_eps[:, t], mv[:, t, 1], EPS, None, ALU.add).then_inc(s_pstep, 1)
                pool.wait_ge(s_pstep, 5 + k)
                pool.tensor_tensor(rstd[:, t], var_eps[:, t], half[:, :], ALU.pow).then_inc(s_rstd, 1)

        def ln_stats(dve, k):
            for t in range(TB):
                n = TB * (k % B) + t
                dve.bn_stats(stats[:, n, :], x_sb[:, n, :]).then_inc(s_st, 1)
            for t in range(TB):
                n = TB * (k % B) + t
                dve.wait_ge(s_st, TB * k + t + 1)
                dve.bn_aggr(mv[:, n, :], stats[:, n, :]).then_inc(s_mv, 1)

        def ln_norm(dve, k):
            dve.wait_ge(s_rstd, k + 1)
            for t in range(TB):
                n = TB * (k % B) + t
                dve.tensor_scalar(xn[:, n, :], x_sb[:, n, :], mv[:, n, 0:1], rstd[:, n:n + 1],
                                  ALU.subtract, ALU.mult).then_inc(s_xn, 1)

        def ln_transpose(pe, k):
            pe.wait_ge(s_xn, TB * (k + 1))
            if k >= 2:
                pe.wait_ge(s_hful, KC * (k - 1))
            for c in range(KC):
                for t in range(TB):
                    last = pe.transpose(ps[:, LNB[k // B] + k % 2, c * N + t * P:c * N + (t + 1) * P],
                                        xn[:, TB * (k % B) + t, c * P:(c + 1) * P], ident[:, :])
            last.then_inc(s_xt, 1)

        LNB = (6, 0)

        def ln_high(act, k):
            b = k % B
            act.wait_ge(s_hful, KC * (k + 1))
            act.activation(h_hi[:, :, b * N:(b + 1) * N], h_full[:, k % 2, :, :], ACT.Copy).then_inc(s_hhi, 1)

        def ln_full(dve, k):
            b, s = k % B, k // B
            dve.wait_ge(s_xt, k + 1)
            if k >= 2:
                dve.wait_ge(s_hlo, k - 1)
            for c in range(KC):
                dve.tensor_scalar(h_full[:, k % 2, c, :], ps[:, LNB[s] + k % 2, c * N:(c + 1) * N],
                                  mod_sb[:, 2 + s, c, b:b + 1], mod_sb[:, s, c, b:b + 1],
                                  ALU.mult, ALU.add).then_inc(s_hful, 1)

        def ln_low(dve, k):
            b = k % B
            dve.wait_ge(s_hhi, k + 1)
            dve.tensor_tensor(h_lo[:, :, b * N:(b + 1) * N], h_full[:, k % 2, :, :],
                              h_hi[:, :, b * N:(b + 1) * N].bitcast(fp32), ALU.subtract).then_inc(s_hlo, 1)

        def products(pe, dst, pairs, start=True, stop=True, skip=False):
            for j, (a, m) in enumerate(pairs):
                last = pe.matmul(dst, a, m, start=start and j == 0, stop=stop and j == len(pairs) - 1,
                                 skip_group_check=skip)
            return last

        def three(a_hi, a_lo, m_hi, m_lo):
            return [(a_hi, m_hi), (a_hi, m_lo), (a_lo, m_hi)]

        def project_out(pe, n):
            pe.wait_ge(s_oth, n + 1)
            pe.wait_ge(s_otl, n + 1)
            if n >= 2:
                pe.wait_ge(s_yb, n - 1)
            pairs = []
            for k in range(KC):
                c = slice(k * P, (k + 1) * P)
                pairs += three(ot_hi[:, n % 2, c], ot_lo[:, n % 2, c], wo_hi[:, k, :], wo_lo[:, k, :])
            products(pe, ps[:, 6 + n % 2, 0:C], pairs).then_inc(s_y, 1)

        @block.tensor
        def _(pe):
            pe.sem_inc(s_projk, 1)
            pe.sem_inc(s_s, 1)
            pe.sem_inc(s_t, SR)
            pe.sem_inc(s_pv, TR)
            pe.wait_ge(s_sc, 1)
            pe.wait_ge(s_wmod, 16)
            for i, m in enumerate((SA, SB, CA, CB)):
                for c in range(KC):
                    col = m * C + c * P
                    o = (i * KC + c) * B
                    last = products(pe, ps[:, 0, o:o + B],
                                    [(wmod_sb[:, k, col:col + P], sc_sb[:, k, :]) for k in range(KC)])
            last.then_inc(s_modp, 1)
            for i, m in enumerate((GA, GB)):
                last = products(pe, ps[0:B, 1, i * C:(i + 1) * C],
                                [(sc_sb[:, k, :], wmod_sb[:, k, m * C:(m + 1) * C]) for k in range(KC)])
            last.then_inc(s_modp, 1)
            pe.wait_ge(s_const, 4)
            for b in range(2):
                ln_transpose(pe, b)
            pe.wait_ge(s_gstep, 5)
            for i in range(2):
                for b in range(B):
                    last = pe.matmul(ps[:, 2 + 2 * i + b // 2, (b % 2) * C:(b % 2 + 1) * C], sel[0:B, b, :],
                                     gate_fin[:, i * C:(i + 1) * C], start=True, stop=True)
            last.then_inc(s_gbp, 1)
            for b in range(2, B):
                ln_transpose(pe, b)
            pe.wait_ge(s_wvs, 2)
            pe.wait_ge(s_mod, 2)
            pe.wait_ge(s_gstep, 1)
            for b in range(B):
                pe.wait_ge(s_hlo, b + 1)
                if b >= 2:
                    pe.wait_ge(s_v, b - 1)
                for t in range(TB):
                    tok = slice((TB * b + t) * P, (TB * b + t + 1) * P)
                    pairs = []
                    for k in range(KC):
                        pairs += three(h_hi[:, k, tok], h_lo[:, k, tok], wv_hi[:, k, :], wv_lo[:, k, :])
                    last = products(pe, ps[:, b % 2, t * C:(t + 1) * C], pairs)
                last.then_inc(s_vp, 1)
            pe.wait_ge(s_v, B)
            pe.wait_ge(s_gb, 1)
            with pe.Fori(0, G) as g:
                pe.wait_ge(s_wqks, g + 1)
                pe.wait_ge(s_ttr, g * UN + 1)
                for m, done in ((0, s_projq), (1, s_projk)):
                    for ch in range(NCH):
                        pairs = []
                        for k in range(KC):
                            w = slice((m * KC + k) * P, (m * KC + k + 1) * P)
                            tok = slice(ch * TC, (ch + 1) * TC)
                            pairs += three(wqk_hi[:, w], wqk_lo[:, w], h_hi[:, k, tok], h_lo[:, k, tok])
                        last = products(pe, ps[:, 2 * m + ch, :], pairs)
                    last.then_inc(done, 1)

                def scores(u):
                    b, pair = u // 2, u % 2
                    if u == 0:
                        pe.wait_ge(s_q, g + 2)
                        pe.wait_ge(s_k, g + 1)
                        pe.wait_ge(s_kd, (g + 1) * 2 * GH * 16 + 16)
                    if u >= 2:
                        pe.wait_ge(s_ttr, g * UN + u)
                    for qt in range(TB):
                        q = q_st[:, b * N + qt * P:b * N + (qt + 1) * P]
                        keys = (qt + 1) * P
                        dst = ps[:, 2 * pair + qt, 0:2 * keys]
                        last = products(pe, dst, [(q, kd[:, 2 * pair:2 * pair + 2, b * N:b * N + keys])
                                                  for kd in (kd_hi, kd_lo)])
                    last.then_inc(s_s, 1)

                def transposes(u):
                    pe.wait_ge(s_exp, g * UN + u + 1)
                    pe.wait_ge(s_pta, g * UN + u + 1)
                    pe.wait_ge(s_ptv, g * UN + u + 1)
                    for j in range(6):
                        last = pe.transpose(ps[:, 4 + j // 3, (j % 3) * P:(j % 3 + 1) * P],
                                            p_sb[:, u % SR, j * P:(j + 1) * P], ident[:, :])
                    last.then_inc(s_t, 1)

                def values(u):
                    b, pair = u // 2, u % 2
                    pe.wait_ge(s_pta, g * UN + u + 2)
                    pe.wait_ge(s_ptv, g * UN + u + 2)
                    pe.wait_ge(s_at, g * UN + u + 1)
                    for i in range(2):
                        first = (2 * pair + i) * HD
                        for qt in range(TB):
                            blocks = [(i, 0)] if qt == 0 else [(2 + 2 * i, 0), (3 + 2 * i, 1)]
                            o = (2 * qt + i) * P
                            last = products(pe, ps[:, 6 + u % 2, o:o + P],
                                            [(p_t[:, u % TR, blk * P:(blk + 1) * P],
                                              v_sb[:, TB * b + kt, ds(g * GH * HD + first, P)]) for blk, kt in blocks])
                    last.then_inc(s_pv, 1)

                for s in range(UN + 3):
                    if s < UN:
                        scores(s)
                    if 0 <= s - 2 < UN:
                        transposes(s - 2)
                    if 0 <= s - 3:
                        values(s - 3)
            for n in range(NT):
                b = n // TB
                if n >= 2:
                    pe.wait_ge(s_otl, n - 1)
                else:
                    pe.wait_ge(s_at, 2 + G * UN)
                for c in range(KC):
                    last = pe.transpose(ps[:, 4 + n % 2, c * P:(c + 1) * P], attn[:, n, c * P:(c + 1) * P], ident[:, :])
                last.then_inc(s_ot, 1)
                if n == 0:
                    pe.wait_ge(s_wos, 2)
                if n >= 1:
                    project_out(pe, n - 1)
                if n % TB == 0 and n >= TB * 2:
                    ln_transpose(pe, B + n // TB - 2)
            project_out(pe, NT - 1)
            for b in range(B - 2, B):
                ln_transpose(pe, B + b)
            pe.wait_ge(s_wrs, 2)
            pe.wait_ge(s_hlo, 2 * B)
            for ch in range(NCH):
                tok = slice(ch * TC, (ch + 1) * TC)
                pairs = []
                for k in range(KC):
                    pairs += three(wr_hi[:, k, :], wr_lo[:, k, :], h_hi[:, k, tok], h_lo[:, k, tok])
                last = products(pe, ps[:, 2 + ch, :], pairs)
            last.then_inc(s_lg, 1)
            pe.wait_ge(s_lgt, 1)
            for n in range(NT):
                last = pe.transpose(ps[:, 2, n * E:(n + 1) * E], lg_t[:, n * P:(n + 1) * P], ident[0:E, 0:E])
            last.then_inc(s_lgs, 1)
            pe.wait_ge(s_rstep, RSTEPS)
            for n in range(NT):
                last = pe.transpose(ps[0:E, 4 + n // 4, (n % 4) * P:(n % 4 + 1) * P], comb[:, n, :], ident[:, :])
            last.then_inc(s_ct, 1)
            pe.wait_ge(s_cts, 1)
            for k in range(E):
                if k >= 2:
                    pe.wait_ge(s_cbs, k - 1)
                for ch in range(NCH):
                    last = pe.matmul(ps[:, 2 * (k % 2) + ch, :], sel[:, k, :], comb_t[:, ch * TC:(ch + 1) * TC],
                                     start=True, stop=True)
                last.then_inc(s_cb, 1)
            pe.wait_ge(s_cbs, E)
            for k in range(4):
                pe.matmul(ps[:, 4 + k, :], zeros[:, 0:P], zeros[:, :], start=True, stop=False, skip_group_check=True)

            def gate_up(first, w, u):
                ch, i = u // IT % NCH, u % IT
                pe.wait_ge(s_au, first + u + 1)
                tok = slice(ch * TC, (ch + 1) * TC)
                for part in range(2):
                    pairs = []
                    for k in range(KC):
                        c = slice(part * UW + k * I + i * P, part * UW + k * I + (i + 1) * P)
                        pairs += three(w_hi[:, w, c], w_lo[:, w, c], h_hi[:, k, tok], h_lo[:, k, tok])
                    last = products(pe, ps[:, 2 * part + u % 2, :], pairs)
                last.then_inc(s_gu, 1)

            def down(first, w, u):
                ch, i = u // IT % NCH, u % IT
                pe.wait_ge(s_al, first + u + 1)
                c = slice(2 * UW + i * C, 2 * UW + (i + 1) * C)
                for t in range(TC // P):
                    n = ch * (TC // P) + t
                    a = slice(t * P, (t + 1) * P)
                    last = products(pe, ps[:, 4 + n // 2, (n % 2) * C:(n % 2 + 1) * C],
                                    three(act_hi[:, u % 2, a], act_lo[:, u % 2, a], w_hi[:, w, c], w_lo[:, w, c]),
                                    start=False, stop=False, skip=True)
                last.then_inc(s_dn, 1)

            with pe.Fori(0, EA // 2) as pair:
                e = pair * 2
                for u in range(2 * UE):
                    w = u // UE
                    if u % UE == 0:
                        pe.wait_ge(s_wh, 3 * (e + w + 1))
                        pe.wait_ge(s_ws, 3 * (e + w + 1))
                    gate_up(e * UE, w, u)
                    if u >= 1:
                        down(e * UE, (u - 1) // UE, u - 1)
                down(e * UE, 1, 2 * UE - 1)
            for k in range(4):
                last = pe.matmul(ps[:, 4 + k, :], zeros[:, 0:P], zeros[:, :], start=False, stop=True, skip_group_check=True)
            last.then_inc(s_fin, 1)

        @block.scalar
        def _(act):
            act.sem_inc(s_pta, 1)
            act.dma_start(ct_sb[:, :, :], c_t).then_inc(s_small, 16)
            act.dma_start(wmod_sb[:, :, :], wmod).then_inc(s_wmod, 16)
            act.dma_start(bqk_sb[:, :, :], bqk).then_inc(s_small, 16)
            act.dma_start(low_sb[:, :], low_rows).then_inc(s_small, 16)
            act.dma_start(bv_b[:, :], bv.partition_broadcast(P)).then_inc(s_small, 16)
            act.dma_start(bo_b[:, :], bo.partition_broadcast(P)).then_inc(s_small, 16)
            act.dma_start(wr_sb[:, :, :], wr).then_inc(s_small, 16)
            act.wait_ge(s_small, 16 * 6)
            act.activation(sc_sb[:, :, :], ct_sb[:, :, :], ACT.Silu).then_inc(s_sc, 1)
            act.activation(wr_hi[:, :, :], wr_sb[:, :, :], ACT.Copy).then_inc(s_wrs, 1)
            act.wait_ge(s_wvl, 16)
            act.activation(wv_hi[:, :, :], wv_raw[:, :, :], ACT.Copy).then_inc(s_wvs, 1)
            act.wait_ge(s_wol, 16)
            act.activation(wo_hi[:, :, :], wo_raw[:, :, :], ACT.Copy).then_inc(s_wos, 1)
            for b in range(B):
                ln_high(act, b)
            act.wait_ge(s_gbp, 1)
            act.activation(ga_b[:, :, :], ps[:, 2:4, :], ACT.Copy).then_inc(s_gb, 1)
            act.activation(gb_b[:, :, :], ps[:, 4:6, :], ACT.Copy).then_inc(s_gb, 1)
            act.wait_ge(s_wqkl, 16)
            with act.Fori(0, G) as g:
                act.wait_ge(s_projk, g + 1)
                act.activation(wqk_hi[:, :], wqk_raw[:, ds(g, 1), :].rearrange("p a w -> p (a w)"),
                               ACT.Copy).then_inc(s_wqkh, 1)
                act.wait_ge(s_projq, g + 1)
                act.wait_ge(s_q, g + 1)
                act.activation(q_sub[:, :], ps[:, 0:2, :].rearrange("p a w -> p (a w)"), ACT.Identity,
                               scale=low_sb[:, 0:1], bias=bqk_sb[:, 1, ds(g, 1)]).then_inc(s_qsub, 1)
                act.wait_ge(s_projk, g + 2)
                act.wait_ge(s_kd, g * 2 * GH * 16 + 16)
                act.activation(k_hi[:, :], ps[:, 2:4, :].rearrange("p a w -> p (a w)"), ACT.Identity,
                               bias=bqk_sb[:, 2, ds(g, 1)]).then_inc(s_khi, 1)

                def exps(u):
                    act.wait_ge(s_nm, g * UN + u + 1)
                    for qt in range(TB):
                        for i in range(2):
                            o = QB[qt] + i * (qt + 1) * P
                            w = p_sb[:, u % SR, o:o + (qt + 1) * P]
                            last = act.activation(w, w, ACT.Exp, scale=SCALE,
                                                  bias=nmax[:, u % SR, 2 * qt + i:2 * qt + i + 1])
                    last.then_inc(s_exp, 1)

                def weights_out(u):
                    act.wait_ge(s_t, g * UN + u + 1 + SR)
                    act.wait_ge(s_pv, g * UN + u + 1)
                    act.activation(p_t[:, u % TR, 0:3 * P], ps[:, 4, 0:3 * P], ACT.Copy).then_inc(s_pta, 1)

                for s in range(UN + 2):
                    if s >= 2:
                        weights_out(s - 2)
                    if s < UN:
                        exps(s)
            for n in range(NT):
                act.wait_ge(s_ot, n + 1)
                if n >= 2:
                    act.wait_ge(s_y, n - 1)
                act.activation(ot_hi[:, n % 2, :], ps[:, 4 + n % 2, 0:KC * P], ACT.Copy).then_inc(s_oth, 1)
                if n % TB == 0 and n >= TB * 2:
                    ln_high(act, B + n // TB - 2)
            for b in range(B - 2, B):
                ln_high(act, B + b)
            act.wait_ge(s_lg, 1)
            act.activation(lg_t[:, :], ps[0:E, 2:4, :].rearrange("p a w -> p (a w)"), ACT.Copy).then_inc(s_lgt, 1)
            act.wait_ge(s_rstep, 1)
            act.activation(rt["e"][:, :, :], rt["z"][:, :, :], ACT.Exp).then_inc(s_re, 1)
            act.wait_ge(s_ct, 1)
            act.activation(comb_t[:, :], ps[0:E, 4:6, :].rearrange("p a w -> p (a w)"), ACT.Copy).then_inc(s_cts, 1)
            for k in range(E):
                act.wait_ge(s_cb, k + 1)
                act.activation(comb_b[:, k, :], ps[:, 2 * (k % 2):2 * (k % 2) + 2, :].rearrange("p a w -> p (a w)"),
                               ACT.Copy).then_inc(s_cbs, 1)

            def split_high(e, w):
                act.wait_ge(s_wl, (e + 1) * 16)
                for a, z in PARTS:
                    act.activation(w_hi[:, w, a:z], w_raw[:, a:z], ACT.Copy).then_inc(s_wh, 1)

            def two_experts(e, last):
                for u in range(2 * UE):
                    act.wait_ge(s_gu, e * UE + u + 1)
                    act.activation(silu_sb[:, u % 2, :], ps[:, u % 2, :], ACT.Silu).then_inc(s_silu, 1)
                    act.wait_ge(s_au, e * UE + u + 3) if last else act.wait_ge(s_af, e * UE + u + 1)
                    act.activation(act_hi[:, u % 2, :], act_f[:, u % 2, :], ACT.Copy).then_inc(s_ah, 1)
                    if u % UE == 1 and not (last and u >= UE):
                        split_high(e + 1 + u // UE, 1 - u // UE)

            split_high(0, 0)
            with act.Fori(0, E // 2) as pair:
                two_experts(pair * 2, False)
            two_experts(EA - 2, True)

        @block.vector
        def _(dve):
            dve.sem_inc(s_ttr, 1)
            dve.wait_ge(s_const, 11)
            dve.sem_inc(s_ptv, 1)
            dve.sem_inc(s_q, 1)
            dve.sem_inc(s_at, TR)
            steps = {}

            def step(ins, s):
                steps[s.name] = steps.get(s.name, 0) + 1
                ins.then_inc(s, 1)
                dve.wait_ge(s, steps[s.name])

            for b in range(B):
                dve.wait_ge(s_xload[b], 16)
                ln_stats(dve, b)
                if b >= 1:
                    ln_norm(dve, b - 1)
            ln_norm(dve, B - 1)
            dve.wait_ge(s_modp, 1)
            ss = 2 * KC * B
            flat = mod_sb[:, :, :, :].rearrange("p a c b -> p (a c b)")
            dve.tensor_copy(flat[:, 0:ss], ps[:, 0, 0:ss]).then_inc(s_mod, 1)
            dve.tensor_scalar(flat[:, ss:2 * ss], ps[:, 0, ss:2 * ss], 1.0, None, ALU.add).then_inc(s_mod, 1)
            dve.wait_ge(s_modp, 2)
            step(dve.tensor_copy(gate_rows[:, :], ps[0:B, 1, :]), s_gstep)
            step(dve.scalar_tensor_tensor(out=gate_abs[:, :], in0=gate_rows[:, :], scalar=-1.0, in1=gate_rows[:, :],
                                          op0=ALU.mult, op1=ALU.max), s_gstep)
            step(dve.tensor_scalar(gate_sign[:, :], gate_rows[:, :], 0.0, 2.0, ALU.is_ge, ALU.mult), s_gstep)
            step(dve.tensor_scalar(gate_sign[:, :], gate_sign[:, :], 1.0, None, ALU.subtract), s_gstep)
            step(dve.scalar_tensor_tensor(out=gate_fin[:, :], in0=gate_abs[:, :], scalar=0.25, in1=gate_sign[:, :],
                                          op0=ALU.max, op1=ALU.mult), s_gstep)
            dve.wait_ge(s_mod, 2)
            dve.wait_ge(s_wrs, 1)
            dve.tensor_tensor(wr_lo[:, :, :], wr_sb[:, :, :], wr_hi[:, :, :].bitcast(fp32), ALU.subtract).then_inc(s_wrs, 1)
            dve.wait_ge(s_wvs, 1)
            dve.tensor_tensor(wv_lo[:, :, :], wv_raw[:, :, :], wv_hi[:, :, :].bitcast(fp32), ALU.subtract).then_inc(s_wvs, 1)
            dve.wait_ge(s_wos, 1)
            dve.tensor_tensor(wo_lo[:, :, :], wo_raw[:, :, :], wo_hi[:, :, :].bitcast(fp32), ALU.subtract).then_inc(s_wos, 1)
            ln_full(dve, 0)
            for b in range(B):
                if b + 1 < B:
                    ln_full(dve, b + 1)
                ln_low(dve, b)
            for b in range(B):
                dve.wait_ge(s_vp, b + 1)
                if b == 0:
                    dve.wait_ge(s_const, 10)
                for t in range(TB):
                    last = dve.tensor_tensor(v_sb[:, TB * b + t, 0:H * HD].rearrange("p (h d) -> p h d", d=HD)[:, :, 0:D],
                                             ps[:, b % 2, t * C:(t + 1) * C].rearrange("p (h d) -> p h d", d=D),
                                             bv_b[:, :].rearrange("p (h d) -> p h d", d=D), ALU.add)
                last.then_inc(s_v, 1)
            with dve.Fori(0, G) as g:
                dve.wait_ge(s_wqkh, g + 1)
                dve.tensor_tensor(wqk_lo[:, :], wqk_raw[:, ds(g, 1), :].rearrange("p a w -> p (a w)"),
                                  wqk_hi[:, :].bitcast(fp32), ALU.subtract).then_inc(s_wqks, 1)
                dve.wait_ge(s_qsub, g + 1)
                dve.wait_ge(s_s, g * UN + 1)
                dve.scalar_tensor_tensor(out=q_st[:, :], in0=ps[:, 0:2, :].rearrange("p a w -> p (a w)"),
                                         scalar=bqk_sb[:, 0, ds(g, 1)], in1=q_sub[:, :].bitcast(fp32),
                                         op0=ALU.add, op1=ALU.subtract).then_inc(s_q, 1)
                dve.wait_ge(s_khi, g + 1)
                dve.wait_ge(s_kd, g * 2 * GH * 16 + 16)
                dve.scalar_tensor_tensor(out=k_lo[:, :], in0=ps[:, 2:4, :].rearrange("p a w -> p (a w)"),
                                         scalar=bqk_sb[:, 2, ds(g, 1)], in1=k_hi[:, :].bitcast(fp32),
                                         op0=ALU.add, op1=ALU.subtract).then_inc(s_k, 1)

                def masked(u):
                    pair = u % 2
                    dve.wait_ge(s_s, g * UN + u + 2)
                    dve.sem_inc(s_own, 1)
                    for qt in range(TB):
                        w = (qt + 1) * P
                        for i in range(2):
                            j = 2 * qt + i
                            last = dve.tensor_tensor_reduce(p_sb[:, u % SR, QB[qt] + i * w:QB[qt] + (i + 1) * w],
                                                            ps[:, 2 * pair + qt, i * w:(i + 1) * w],
                                                            mask[:, qt * P:qt * P + w], 1.0, FLOOR, ALU.add, ALU.max,
                                                            rmax[:, u % SR, j:j + 1])
                    last.then_inc(s_ttr, 1)
                    dve.wait_ge(s_ttr, g * UN + u + 2)
                    dve.tensor_scalar(nmax[:, u % SR, :], rmax[:, u % SR, :], -SCALE, None, ALU.mult).then_inc(s_nm, 1)

                def weights_out(u):
                    dve.wait_ge(s_t, g * UN + u + 1 + SR)
                    dve.wait_ge(s_pv, g * UN + u + 1)
                    dve.tensor_copy(p_t[:, u % TR, 3 * P:6 * P], ps[:, 5, 0:3 * P]).then_inc(s_ptv, 1)

                def normalise(u):
                    b, pair = u // 2, u % 2
                    dve.wait_ge(s_pv, g * UN + u + 1 + TR)
                    o = ps[:, 6 + u % 2, :].rearrange("p (q h d) -> p q h d", q=TB, h=2)
                    dve.reciprocal(rsum[:, u % TR, :].rearrange("p (q h) -> p q h", q=TB), o[:, :, :, D]).then_inc(s_rs, 1)
                    dve.wait_ge(s_rs, g * UN + u + 1)
                    for qt in range(TB):
                        last = dve.tensor_tensor(
                            attn[:, TB * b + qt, ds(g * GH * D + pair * 2 * D, 2 * D)].rearrange("p (h d) -> p h d", d=D),
                            o[:, qt, :, 0:D],
                            rsum[:, u % TR, 2 * qt:2 * qt + 2].unsqueeze(2).to_broadcast([P, 2, D]), ALU.mult)
                    last.then_inc(s_at, 1)

                for s in range(UN + 4):
                    if s < UN:
                        masked(s)
                    if 0 <= s - 2 < UN:
                        weights_out(s - 2)
                    if s >= 4:
                        normalise(s - 4)

            def residual(n):
                b = n // TB
                dve.wait_ge(s_y, n + 1)
                if n >= 2:
                    dve.wait_ge(s_yg, n - 1)
                dve.tensor_tensor(y_sb[:, n % 2, :], ps[:, 6 + n % 2, 0:C], bo_b[:, :], ALU.add).then_inc(s_yb, 1)
                dve.wait_ge(s_yb, n + 1)
                if n >= 2:
                    dve.wait_ge(s_x2, n - 1)
                dve.tensor_tensor(y_gated[:, n % 2, :], y_sb[:, n % 2, :], ga_b[:, b, :], ALU.mult).then_inc(s_yg, 1)
                dve.wait_ge(s_yg, n + 1)
                dve.tensor_tensor(x_sb[:, n, :], x_sb[:, n, :], y_gated[:, n % 2, :], ALU.add).then_inc(s_x2, 1)
                dve.wait_ge(s_x2, n + 1)

            for n in range(NT):
                dve.wait_ge(s_oth, n + 1)
                if n >= 2:
                    dve.wait_ge(s_y, n - 1)
                dve.tensor_tensor(ot_lo[:, n % 2, :], ps[:, 4 + n % 2, 0:KC * P],
                                  ot_hi[:, n % 2, :].bitcast(fp32), ALU.subtract).then_inc(s_otl, 1)
                if n >= 1:
                    residual(n - 1)
                if n % TB == 0 and n >= TB:
                    k = B + n // TB - 1
                    ln_stats(dve, k)
                    ln_norm(dve, k)
                if n % TB == 0 and n >= 2 * TB:
                    ln_full(dve, B + n // TB - 2)
                    ln_low(dve, B + n // TB - 2)
            residual(NT - 1)
            ln_stats(dve, 2 * B - 1)
            ln_norm(dve, 2 * B - 1)
            ln_full(dve, 2 * B - 2)
            ln_full(dve, 2 * B - 1)
            ln_low(dve, 2 * B - 2)
            ln_low(dve, 2 * B - 1)
            last8 = lambda v: v.unsqueeze(2).to_broadcast([P, NT, E])
            dve.wait_ge(s_lgs, 1)
            R = s_rstep
            dve.wait_ge(s_const, 11)
            step(dve.tensor_scalar(rt["z"][:, :, :], ps[:, 2, 0:NT * E].rearrange("p (n e) -> p n e", e=E), -1.0, EXP_MAX,
                                   ALU.mult, ALU.min), R)
            dve.wait_ge(s_re, 1)
            step(dve.tensor_scalar(rt["p"][:, :, :], rt["e"][:, :, :], 1.0, None, ALU.add), R)
            step(dve.reciprocal(rt["s"][:, :, :], rt["p"][:, :, :]), R)
            src = rt["s"]
            for j in ("1", "2"):
                step(dve.tensor_reduce(rv["v" + j][:, :], src[:, :, :], AX.X, ALU.max), R)
                step(dve.tensor_tensor(rt["eq" + j][:, :, :], src[:, :, :], last8(rv["v" + j][:, :]), ALU.is_equal), R)
                step(dve.tensor_tensor(rt["t" + j][:, :, :], rt["eq" + j][:, :, :], cand[:, :, :], ALU.mult), R)
                step(dve.tensor_reduce(rv["i" + j][:, :], rt["t" + j][:, :, :], AX.X, ALU.min), R)
                step(dve.tensor_tensor(rt["m" + j][:, :, :], cand[:, :, :], last8(rv["i" + j][:, :]), ALU.is_equal), R)
                if j == "1":
                    step(dve.scalar_tensor_tensor(out=rt["s2"][:, :, :], in0=rt["m1"][:, :, :], scalar=-2.0,
                                                  in1=rt["s"][:, :, :], op0=ALU.mult, op1=ALU.add), R)
                    src = rt["s2"]
            step(dve.tensor_tensor(rv["den"][:, :], rv["v1"][:, :], rv["v2"][:, :], ALU.add), R)
            step(dve.reciprocal(rv["rden"][:, :], rv["den"][:, :]), R)
            step(dve.tensor_tensor(rt["m"][:, :, :], rt["m1"][:, :, :], rt["m2"][:, :, :], ALU.add), R)
            step(dve.tensor_tensor(rt["c"][:, :, :], rt["m"][:, :, :], rt["s"][:, :, :], ALU.mult), R)
            step(dve.tensor_tensor(comb[:, :, :], rt["c"][:, :, :], last8(rv["rden"][:, :]), ALU.mult), R)
            assert steps[R.name] == RSTEPS, steps

            dve.sem_inc(s_au, 2)
            def split_low(e, w):
                for j, (a, z) in enumerate(PARTS):
                    dve.wait_ge(s_wh, 3 * e + j + 1)
                    dve.tensor_tensor(w_lo[:, w, a:z], w_raw[:, a:z], w_hi[:, w, a:z].bitcast(fp32),
                                      ALU.subtract).then_inc(s_ws, 1)

            def two_experts(e, last):
                for u in range(2 * UE):
                    first = e * UE + u
                    ch = u // IT % NCH
                    dve.wait_ge(s_silu, first + 1)
                    if last:
                        dve.tensor_tensor(act_f[:, u % 2, :], silu_sb[:, u % 2, :], ps[:, 2 + u % 2, :],
                                          ALU.mult).then_inc(s_au, 1)
                    else:
                        dve.tensor_tensor(act_u[:, u % 2, :], silu_sb[:, u % 2, :], ps[:, 2 + u % 2, :],
                                          ALU.mult).then_inc(s_au, 1)
                        dve.wait_ge(s_au, first + 3)
                        dve.tensor_tensor(act_f[:, u % 2, :], act_u[:, u % 2, :],
                                          comb_b[:, ds(e + u // UE, 1), ch * TC:(ch + 1) * TC].rearrange("p a t -> p (a t)"),
                                          ALU.mult).then_inc(s_af, 1)
                    dve.wait_ge(s_ah, first + 1)
                    dve.tensor_tensor(act_lo[:, u % 2, :], act_f[:, u % 2, :], act_hi[:, u % 2, :].bitcast(fp32),
                                      ALU.subtract).then_inc(s_al, 1)
                    if u % UE == 1 and not (last and u >= UE):
                        split_low(e + 1 + u // UE, 1 - u // UE)

            split_low(0, 0)
            with dve.Fori(0, E // 2) as pair:
                two_experts(pair * 2, False)
            two_experts(EA - 2, True)
            dve.wait_ge(s_fin, 1)
            for n in range(NT):
                if n >= 2:
                    dve.wait_ge(s_out[n % 2], 16 * (n // 2))
                dve.tensor_tensor(res[:, n % 2, :], ps[:, 4 + n // 2, (n % 2) * C:(n % 2 + 1) * C],
                                  gb_b[:, n // TB, :], ALU.mult).then_inc(s_resg, 1)
                dve.wait_ge(s_resg, n + 1)
                dve.tensor_tensor(res[:, n % 2, :], res[:, n % 2, :], x_sb[:, n, :], ALU.add).then_inc(s_res, 1)


def kernel(**inputs):
    import numpy as np
    import concourse.bacc as bacc
    from concourse.bass_utils import run_bass_kernel_spmd as run

    a = {k.removeprefix("L0_"): np.asarray(v) for k, v in inputs.items()}

    def by_rows(w):
        return w.reshape(-1, P, w.shape[1]).transpose(1, 0, 2)

    def strips(w):
        w = w.reshape(G, GH, 1, D, *w.shape[1:])
        return np.concatenate([w, w], axis=2).reshape(G, GH * 2 * D, *w.shape[4:])

    wq, wk = (strips(a["attn_W" + n]) for n in "qk")
    wqk = np.stack([wq, wk], 1).reshape(G, 2, P, KC, P).transpose(4, 0, 1, 3, 2)
    bq, bk = (strips(a["attn_b" + n].reshape(H * D)) for n in "qk")
    low = np.tile(np.repeat(np.array([0.0, 1.0], np.float32), D), GH)
    bq_low = np.where(low[None] > 0, bq, np.zeros_like(bq))
    arrays = {
        "x": a["attn_x"].reshape(T, C),
        "c_t": a["c"].T.reshape(KC, P, B).transpose(1, 0, 2),
        "wmod": by_rows(a["wmod"]),
        "wqk": wqk.reshape(P, G, 2 * KC * P),
        "bqk": np.stack([bq.T, bq_low.T, bk.T], 1),
        "low_rows": low[:, None],
        "wv": by_rows(a["attn_Wv"].T),
        "bv": a["attn_bv"],
        "wo": by_rows(a["attn_Wo"].T),
        "bo": a["attn_bo"],
        "wr": by_rows(np.concatenate([a["ffn_w_router"].T, np.zeros((C, P - E), a["ffn_w_router"].dtype)], 1)),
    }

    def expert(g, u, d):
        return np.concatenate([by_rows(m.T).reshape(P, -1) for m in (g, u, d)], 1)

    arrays["experts"] = np.stack(
        [expert(a["ffn_wg"][e], a["ffn_wu"][e], a["ffn_wd"][e]) for e in range(E)]
        + [expert(a["ffn_sg"][j], a["ffn_su"][j], a["ffn_sd"][j]) for j in range(NSH)])

    nc = bacc.Bacc("TRN2", target_bir_lowering=False, num_devices=1)
    arrays = {f"in_{k}": np.ascontiguousarray(v) for k, v in arrays.items()}
    args = [nc.dram_tensor(k, v.shape, mybir.dt.from_np(v.dtype), kind="ExternalInput").ap() for k, v in arrays.items()]
    out = nc.dram_tensor("out_x", (T, C), mybir.dt.float32, kind="ExternalOutput").ap()
    adaln_block_kernel(nc, *args, out)
    r = run(nc, [arrays], core_ids=[0])
    return r.results[0]["out_x"].reshape(B, N, C)
```
